# Optimizing a Trainium2 kernel written in Bass

```python
import numpy as np
import jax
import jax.numpy as jnp

def _softmax(x, axis=-1):
    return jax.nn.softmax(x, axis=axis)

def _gelu(x):
    return jax.nn.gelu(x, approximate=True)

def _silu(x):
    return jax.nn.silu(x)

def _sigmoid(x):
    return jax.nn.sigmoid(x)

def _layernorm(x, axis=-1, eps=1e-05):
    m = jnp.mean(x, axis=axis, keepdims=True)
    v = jnp.var(x, axis=axis, keepdims=True)
    return (x - m) / jnp.sqrt(v + eps)

def _scatter_add(tgt, idx, src, axis=0):
    return tgt.at[idx].add(src)

def _segment_sum(src, seg, n):
    return jax.ops.segment_sum(src, seg, n)
kernel_name = 'mk_seq_postln_d1_jaxref_r4_dea2df'

def setup_inputs(seed: int=0):
    np.random.seed(seed)
    _w = jnp.asarray

    def _L0_attn_setup():
        import jax, jax.numpy as jnp
        import numpy as np
        C_CONST = 8.0
        EPS = 1e-06
        K = 4

        def rmsnorm(x, w):
            var = jnp.mean(x * x, axis=-1, keepdims=True)
            return x * jax.lax.rsqrt(var + EPS) * w

        def causal_depthwise_conv(x, conv_w, conv_b):
            B, S, D = x.shape
            xp = jnp.pad(x, ((0, 0), (K - 1, 0), (0, 0)))
            out = conv_b
            for k in range(K):
                out = out + conv_w[k] * xp[:, k:k + S, :]
            return out

        def rg_lru(x, Wi, Wa, lam):
            r = jax.nn.sigmoid(jnp.einsum('bsd,de->bse', x, Wa))
            i = jax.nn.sigmoid(jnp.einsum('bsd,de->bse', x, Wi))
            log_a = -C_CONST * jax.nn.softplus(lam) * r
            a = jnp.exp(log_a)
            b = jnp.sqrt(jnp.maximum(1.0 - a * a, 1e-12)) * (i * x)

            def comb(e1, e2):
                a1, b1 = e1
                a2, b2 = e2
                return (a1 * a2, a2 * b1 + b2)
            _, h = jax.lax.associative_scan(comb, (a, b), axis=1)
            return h
        key = jax.random.key(seed)
        ks = jax.random.split(key, 16)
        B, S, D, H = (4, 512, 256, 1024)
        s = 0.02
        return {'x': jax.random.normal(ks[0], (B, S, D), jnp.float32), 'norm1_w': jnp.ones((D,), jnp.float32), 'Wx': jax.random.normal(ks[1], (D, D), jnp.float32) * s, 'Wy': jax.random.normal(ks[2], (D, D), jnp.float32) * s, 'conv_w': jax.random.normal(ks[3], (K, D), jnp.float32) * s, 'conv_b': jnp.zeros((D,), jnp.float32), 'Wi': jax.random.normal(ks[4], (D, D), jnp.float32) * s, 'Wa': jax.random.normal(ks[5], (D, D), jnp.float32) * s, 'lam': jax.random.normal(ks[6], (D,), jnp.float32) * 0.5, 'Wo': jax.random.normal(ks[7], (D, D), jnp.float32) * s, 'norm2_w': jnp.ones((D,), jnp.float32), 'Wg': jax.random.normal(ks[8], (D, H), jnp.float32) * s, 'Wu': jax.random.normal(ks[9], (D, H), jnp.float32) * s, 'Wd': jax.random.normal(ks[10], (H, D), jnp.float32) * s}
    _L0_attn_in = _L0_attn_setup()

    def _L0_ffn_setup():
        import jax, jax.numpy as jnp
        import numpy as np
        HIDDEN = 256
        INTER = 1024
        key = jax.random.key(seed)
        k1, k2, k3, k4, k5 = jax.random.split(key, 5)
        hidden_states = jax.random.normal(k1, (4, 512, HIDDEN), dtype=jnp.float32)
        W1 = jax.random.normal(k2, (HIDDEN, INTER), dtype=jnp.float32) * (1.0 / np.sqrt(HIDDEN))
        b1 = jax.random.normal(k3, (INTER,), dtype=jnp.float32) * 0.02
        W2 = jax.random.normal(k4, (INTER, HIDDEN), dtype=jnp.float32) * (1.0 / np.sqrt(INTER))
        b2 = jax.random.normal(k5, (HIDDEN,), dtype=jnp.float32) * 0.02
        return {'hidden_states': hidden_states, 'W1': W1, 'b1': b1, 'W2': W2, 'b2': b2}
    _L0_ffn_in = _L0_ffn_setup()
    _d = {'L0_attn_x': _L0_attn_in['x'], 'L0_attn_norm1_w': _L0_attn_in['norm1_w'], 'L0_attn_Wx': _L0_attn_in['Wx'], 'L0_attn_Wy': _L0_attn_in['Wy'], 'L0_attn_conv_w': _L0_attn_in['conv_w'], 'L0_attn_conv_b': _L0_attn_in['conv_b'], 'L0_attn_Wi': _L0_attn_in['Wi'], 'L0_attn_Wa': _L0_attn_in['Wa'], 'L0_attn_lam': _L0_attn_in['lam'], 'L0_attn_Wo': _L0_attn_in['Wo'], 'L0_attn_norm2_w': _L0_attn_in['norm2_w'], 'L0_attn_Wg': _L0_attn_in['Wg'], 'L0_attn_Wu': _L0_attn_in['Wu'], 'L0_attn_Wd': _L0_attn_in['Wd'], 'L0_ffn_W1': _L0_ffn_in['W1'], 'L0_ffn_b1': _L0_ffn_in['b1'], 'L0_ffn_W2': _L0_ffn_in['W2'], 'L0_ffn_b2': _L0_ffn_in['b2']}
    _x0 = _d['L0_attn_x']
    _d['L0_attn_x'] = jax.random.normal(jax.random.fold_in(jax.random.key(seed), 1), (4, 1024, 256), dtype=_x0.dtype)
    del _x0
    return _d

def reference(L0_attn_x, L0_attn_norm1_w, L0_attn_Wx, L0_attn_Wy, L0_attn_conv_w, L0_attn_conv_b, L0_attn_Wi, L0_attn_Wa, L0_attn_lam, L0_attn_Wo, L0_attn_norm2_w, L0_attn_Wg, L0_attn_Wu, L0_attn_Wd, L0_ffn_W1, L0_ffn_b1, L0_ffn_W2, L0_ffn_b2):

    def _L0_attn_ref(x, norm1_w, Wx, Wy, conv_w, conv_b, Wi, Wa, lam, Wo, norm2_w, Wg, Wu, Wd):
        import jax, jax.numpy as jnp
        import numpy as np
        C_CONST = 8.0
        EPS = 1e-06
        K = 4

        def rmsnorm(x, w):
            var = jnp.mean(x * x, axis=-1, keepdims=True)
            return x * jax.lax.rsqrt(var + EPS) * w

        def causal_depthwise_conv(x, conv_w, conv_b):
            B, S, D = x.shape
            xp = jnp.pad(x, ((0, 0), (K - 1, 0), (0, 0)))
            out = conv_b
            for k in range(K):
                out = out + conv_w[k] * xp[:, k:k + S, :]
            return out

        def rg_lru(x, Wi, Wa, lam):
            r = jax.nn.sigmoid(jnp.einsum('bsd,de->bse', x, Wa))
            i = jax.nn.sigmoid(jnp.einsum('bsd,de->bse', x, Wi))
            log_a = -C_CONST * jax.nn.softplus(lam) * r
            a = jnp.exp(log_a)
            b = jnp.sqrt(jnp.maximum(1.0 - a * a, 1e-12)) * (i * x)

            def comb(e1, e2):
                a1, b1 = e1
                a2, b2 = e2
                return (a1 * a2, a2 * b1 + b2)
            _, h = jax.lax.associative_scan(comb, (a, b), axis=1)
            return h
        t = rmsnorm(x, norm1_w)
        xb = jnp.einsum('bsd,de->bse', t, Wx)
        xb = causal_depthwise_conv(xb, conv_w, conv_b)
        h = rg_lru(xb, Wi, Wa, lam)
        yb = jax.nn.gelu(jnp.einsum('bsd,de->bse', t, Wy))
        mix = jnp.einsum('bsd,de->bse', h * yb, Wo)
        h1 = x + mix
        u = rmsnorm(h1, norm2_w)
        ffn = jnp.einsum('bsh,hd->bsd', jax.nn.gelu(jnp.einsum('bsd,dh->bsh', u, Wg)) * jnp.einsum('bsd,dh->bsh', u, Wu), Wd)
        return h1 + ffn

    def _L0_ffn_ref(hidden_states, W1, b1, W2, b2):
        import jax, jax.numpy as jnp
        import numpy as np
        HIDDEN = 256
        INTER = 1024
        h = jax.nn.relu(jnp.einsum('bsh,hi->bsi', hidden_states, W1) + b1)
        return jnp.einsum('bsi,ih->bsh', h, W2) + b2
    x = L0_attn_x
    x = _layernorm(x + _L0_attn_ref(x, L0_attn_norm1_w, L0_attn_Wx, L0_attn_Wy, L0_attn_conv_w, L0_attn_conv_b, L0_attn_Wi, L0_attn_Wa, L0_attn_lam, L0_attn_Wo, L0_attn_norm2_w, L0_attn_Wg, L0_attn_Wu, L0_attn_Wd), axis=-1)
    x = _layernorm(x + _L0_ffn_ref(x, L0_ffn_W1, L0_ffn_b1, L0_ffn_W2, L0_ffn_b2), axis=-1)
    return x

_drawn_inputs = setup_inputs


def setup_inputs(seed=0):
    import zlib

    import numpy as np

    out = dict(_drawn_inputs(seed))
    spreads = {'L0_attn_norm1_w': (1.0, 0.6), 'L0_attn_conv_b': (0.0, 0.8), 'L0_attn_norm2_w': (1.0, 0.6)}
    factors = {'L0_attn_Wx': 8.0,
     'L0_attn_Wy': 8.0,
     'L0_attn_conv_w': 8.0,
     'L0_attn_Wi': 8.0,
     'L0_attn_Wa': 8.0,
     'L0_attn_lam': 8.0,
     'L0_attn_Wo': 8.0,
     'L0_attn_Wg': 2.839,
     'L0_attn_Wu': 2.763,
     'L0_attn_Wd': 2.76,
     'L0_ffn_b1': 4.96,
     'L0_ffn_b2': 3.532}
    for name, (base, spread) in spreads.items():
        noise = np.random.default_rng([zlib.crc32(name.encode()), seed]).standard_normal(out[name].shape)
        drawn = base * np.exp(spread * noise) if base else spread * noise
        out[name] = jnp.asarray(drawn.astype(out[name].dtype))
    for name, factor in factors.items():
        out[name] = (out[name] * factor).astype(out[name].dtype)
    return out
```

```python
from contextlib import ExitStack

import concourse.bass as bass
from concourse import mybir


FP32 = mybir.dt.float32
FP32R = mybir.dt.float32r
ACT = mybir.ActivationFunctionType
ALU = mybir.AluOpType

P = 128
T = 512
TT = T // P
TAPS = 4
LOOKBACK = TAPS - 1
RMS_EPS = 1e-6
LN_EPS = 1e-5
C_CONST = 8.0
GATE_FLOOR = 1e-12
RING = 4
DMA = 16


def at(chunk, per_chunk, n):
    pair, k = chunk
    return pair * (2 * per_chunk) + (k * per_chunk + n)


def before(chunk):
    pair, k = chunk
    return pair, k - 1


def after(chunk):
    pair, k = chunk
    return pair, k + 1


def griffin_mlp_kernel(nc, x, norm1_w, Wx, Wy, conv_w, conv_b, Wi, Wa, lam, Wo, norm2_w, Wg, Wu, Wd,
                       W1, b1, W2, b2, out):
    B, S, D = x.shape
    H = Wg.shape[1]
    KD = D // P
    KH = H // P
    PAIRS = TT // 2
    CHUNKS = B * S // T
    assert S == 2 * T and KD == 2 and 2 * D == T and KH == 2 * RING

    x_dram = x.rearrange("b s d -> (b s) d").rearrange("(c t p) d -> c p t d", t=TT, p=P)
    out_dram = out.rearrange("b s d -> (b s) d").rearrange("(c t p) d -> c p t d", t=2, p=P)

    ctx = ExitStack()
    with ctx:
        def sb(name, shape, dt=FP32):
            return ctx.enter_context(nc.sbuf_tensor(name, shape, dt))

        def sem(name):
            return ctx.enter_context(nc.semaphore(name))

        dram = {"x": Wx, "y": Wy, "a": Wa, "i": Wi, "o": Wo, "g": Wg, "u": Wu, "d": Wd, "1": W1, "2": W2}
        w_hi, w_lo = {}, {}
        for n, w in dram.items():
            w_hi[n] = sb(f"w_{n}_hi", [P, w.shape[0] // P, w.shape[1]], FP32R)
            w_lo[n] = sb(f"w_{n}_lo", [P, w.shape[0] // P, w.shape[1]], FP32R)

        VECS = {"n1": 0, "cb": 2, "lam": 4, "n2": 6, "cw": 8, "b1": 16}
        NV = 16 + KH
        vec_rows = sb("vec_rows", [NV, P])
        vecs = sb("vecs", [P, NV])
        ident = sb("ident", [P, P])
        b2_rows = sb("b2_rows", [P, D])
        minus_half = sb("minus_half", [P, TT])
        half_c = sb("half_c", [P, KD])
        sp = sb("sp", [P, 5, KD])

        xs = [sb(f"xs{i}", [P, TT, D]) for i in range(2)]
        normed = sb("normed", [P, TT, D])
        h1 = sb("h1", [P, TT, D])
        row = sb("row", [P, TT, D])
        ss1 = sb("ss1", [P, TT])
        ss2 = sb("ss2", [P, TT])
        rstd1 = sb("rstd1", [P, TT])
        rstd2 = sb("rstd2", [P, TT])
        ln_stats = sb("ln_stats", [P, TT, 6])
        ln_mv = sb("ln_mv", [P, TT, 2])
        ln_rstd = sb("ln_rstd", [P, TT])

        tT_hi = sb("tT_hi", [P, KD, T], FP32R)
        tT_lo = sb("tT_lo", [P, KD, T], FP32R)
        mT_hi = sb("mT_hi", [P, KD, T], FP32R)
        mT_lo = sb("mT_lo", [P, KD, T], FP32R)
        uT_hi = sb("uT_hi", [P, KD, T], FP32R)
        uT_lo = sb("uT_lo", [P, KD, T], FP32R)
        xv = sb("xv", [P, KD, LOOKBACK + T])
        xb = sb("xb", [P, KD, T])
        decay = sb("decay", [P, KD, T])
        inp = sb("inp", [P, KD, T])
        gy = sb("gy", [P, KD, T])
        xtail = sb("xtail", [P, KD, LOOKBACK])
        h_last = sb("h_last", [P, KD])
        ring = sb("ring", [P, RING, T])

        psum = [ctx.enter_context(nc.psum_tensor(f"psum{i}", [P, T], FP32)) for i in range(8)]

        def vec(name, m):
            return vecs[:, VECS[name] + m:VECS[name] + m + 1]

        vecs_loaded = sem("vecs_loaded")
        b2_loaded = sem("b2_loaded")
        w_loaded = {n: sem(f"w_{n}_loaded") for n in dram}
        hi_split = {n: sem(f"w_{n}_hi_split") for n in dram}
        lo_split = {n: sem(f"w_{n}_lo_split") for n in dram}
        ident_zero = sem("ident_zero")
        ident_ready = sem("ident_ready")
        consts_ready = sem("consts_ready")
        vecs_transposed = sem("vecs_transposed")
        vecs_ready = sem("vecs_ready")
        lam_step = sem("lam_step")
        lam_abs = sem("lam_abs")
        lam_exp = sem("lam_exp")
        x_loaded = [sem(f"x_loaded{i}") for i in range(2)]
        out_stored = sem("out_stored")
        x_squared = sem("x_squared")
        rms1_ms = sem("rms1_ms")
        rms1_rstd = sem("rms1_rstd")
        t_ready = sem("t_ready")
        tT_done = sem("tT_done")
        tT_hi_ready = sem("tT_hi_ready")
        tT_lo_ready = sem("tT_lo_ready")
        wx_done = sem("wx_done")
        xhead_ready = sem("xhead_ready")
        xraw_ready = sem("xraw_ready")
        xtail_saved = sem("xtail_saved")
        tap_done = sem("tap_done")
        taps_added = sem("taps_added")
        xb_hi_ready = sem("xb_hi_ready")
        xb_lo_ready = sem("xb_lo_ready")
        wa_done = sem("wa_done")
        wi_done = sem("wi_done")
        wy_done = sem("wy_done")
        tanh_a_ready = sem("tanh_a_ready")
        tanh_i_ready = sem("tanh_i_ready")
        a_ready = sem("a_ready")
        a_squared = sem("a_squared")
        gate_room = sem("gate_room")
        gate_ready = sem("gate_ready")
        ix_ready = sem("ix_ready")
        b_ready = sem("b_ready")
        h_ready = sem("h_ready")
        h_saved = sem("h_saved")
        gy_ready = sem("gy_ready")
        hy_ready = sem("hy_ready")
        hy_hi_ready = sem("hy_hi_ready")
        hy_lo_ready = sem("hy_lo_ready")
        wo_done = sem("wo_done")
        h1_ready = sem("h1_ready")
        h1_squared = sem("h1_squared")
        rms2_ms = sem("rms2_ms")
        rms2_rstd = sem("rms2_rstd")
        u_ready = sem("u_ready")
        xh_ready = sem("xh_ready")
        uT_done = sem("uT_done")
        uT_hi_ready = sem("uT_hi_ready")
        uT_lo_ready = sem("uT_lo_ready")
        gate_done = sem("gate_done")
        up_done = sem("up_done")
        gelu_ready = sem("gelu_ready")
        gu_ready = sem("gu_ready")
        gu_hi_ready = sem("gu_hi_ready")
        gu_lo_ready = sem("gu_lo_ready")
        wd_done = sem("wd_done")
        s1_ready = sem("s1_ready")
        x1_ready = sem("x1_ready")
        x1T_done = sem("x1T_done")
        x1T_hi_ready = sem("x1T_hi_ready")
        x1T_lo_ready = sem("x1T_lo_ready")
        b2_added = sem("b2_added")
        w1_done = sem("w1_done")
        relu_ready = sem("relu_ready")
        hid_hi_ready = sem("hid_hi_ready")
        hid_lo_ready = sem("hid_lo_ready")
        w2_done = sem("w2_done")
        s2_ready = sem("s2_ready")
        out_ready = sem("out_ready")
        pool_carried = sem("pool_carried")
        dve_carried = sem("dve_carried")
        bn_done = [sem(f"bn{i}_done") for i in (1, 2)]
        mv_done = [sem(f"mv{i}_done") for i in (1, 2)]
        ve_done = [sem(f"ve{i}_done") for i in (1, 2)]
        ln_rstd_ready = [sem(f"ln{i}_rstd_ready") for i in (1, 2)]

        with nc.sbuf_tensor("raw_weights", [P, 4, KD * H], FP32) as raw:
            pass
        units_hi = sb("units_hi", [P, KH, T], FP32R)
        units_lo = sb("units_lo", [P, KH, T], FP32R)
        DD = KD * D
        raw_of = {
            "x": raw[:, 0, 0:DD], "y": raw[:, 0, DD:2 * DD], "a": raw[:, 0, 2 * DD:3 * DD],
            "i": raw[:, 0, 3 * DD:4 * DD], "o": row[:, 0:2, :].rearrange("p t d -> p (t d)"),
            "g": raw[:, 1, :], "u": raw[:, 2, :], "d": raw[:, 3, :], "1": raw[:, 0, :], "2": raw[:, 1, :],
        }

        def raw_w(n, k):
            width = dram[n].shape[1]
            return raw_of[n][:, k * width:(k + 1) * width]

        block = ctx.enter_context(nc.Block())

        @block.sync
        def _(sync):
            def load_x(chunk):
                pair, k = chunk
                sync.dma_start(xs[k % 2][:, :, :],
                               x_dram[bass.ds(pair * 2 + k, 1), :, :, :].rearrange("c p t d -> (c p) t d")
                               ).then_inc(x_loaded[k % 2], DMA)

            def load_w(n):
                kt = dram[n].shape[0] // P
                sync.dma_start(raw_of[n].rearrange("p (k n) -> p k n", k=kt),
                               dram[n].rearrange("(k p) n -> p k n", p=P)).then_inc(w_loaded[n], DMA)

            def store_out(chunk):
                pair, k = chunk
                for q in range(PAIRS):
                    sync.wait_ge(out_ready, at(chunk, 4, 2 * q + 2))
                    sync.dma_start(out_dram[bass.ds(pair * (2 * PAIRS) + (k * PAIRS + q), 1), :, :, :]
                                   .rearrange("c p t d -> (c p) t d"),
                                   row[:, 2 * q:2 * q + 2, :]).then_inc(out_stored, DMA)

            sync.sem_inc(out_stored, DMA)
            load_x((0, 0))
            for src, name, rows in ((norm1_w, "n1", KD), (conv_b, "cb", KD), (lam, "lam", KD),
                                    (norm2_w, "n2", KD), (b1, "b1", KH)):
                sync.dma_start(vec_rows[VECS[name]:VECS[name] + rows, :],
                              src.rearrange("(k p) -> k p", p=P)).then_inc(vecs_loaded, DMA)
            sync.dma_start(vec_rows[VECS["cw"]:VECS["cw"] + TAPS * KD, :],
                          conv_w.rearrange("t (k p) -> (t k) p", p=P)).then_inc(vecs_loaded, DMA)
            for n in ("x", "y", "a", "i", "g", "u", "o", "d"):
                load_w(n)
            load_x((0, 1))
            sync.dma_start(b2_rows[:, :], b2.partition_broadcast(P)).then_inc(b2_loaded, DMA)

            for n in ("x", "y", "a", "i"):
                sync.wait_ge(hi_split[n], KD)
                sync.wait_ge(lo_split[n], KD)
            load_w("1")
            sync.wait_ge(hi_split["g"], KD)
            sync.wait_ge(lo_split["g"], KD)
            load_w("2")

            def period(chunk, more):
                if more:
                    sync.wait_ge(s1_ready, at(chunk, 2, 2))
                    load_x(after(after(chunk)))
                store_out(chunk)

            with sync.Fori(0, CHUNKS // 2 - 1) as pair:
                period((pair, 0), True)
                period((pair, 1), True)
            period((CHUNKS // 2 - 1, 0), False)
            period((CHUNKS // 2 - 1, 1), False)
            sync.wait_ge(out_stored, DMA + CHUNKS * PAIRS * DMA)

        @block.tensor
        def _(pe):
            def product(dst, n, m, hi, lo):
                for k in range(KD):
                    cols = slice(m * P, (m + 1) * P)
                    nc.tensor.matmul(dst, w_hi[n][:, k, cols], hi[:, k, :], start=(k == 0), stop=False)
                    nc.tensor.matmul(dst, w_hi[n][:, k, cols], lo[:, k, :], start=False, stop=False)
                    last = nc.tensor.matmul(dst, w_lo[n][:, k, cols], hi[:, k, :],
                                            start=False, stop=(k == KD - 1))
                return last

            def product_by_tokens(dst, n, tt, hi, lo):
                tiles = dram[n].shape[0] // P
                for k in range(tiles):
                    toks = slice(tt * P, (tt + 1) * P)
                    nc.tensor.matmul(dst, hi[:, k, toks], w_hi[n][:, k, :], start=(k == 0), stop=False)
                    nc.tensor.matmul(dst, hi[:, k, toks], w_lo[n][:, k, :], start=False, stop=False)
                    last = nc.tensor.matmul(dst, lo[:, k, toks], w_hi[n][:, k, :],
                                            start=False, stop=(k == tiles - 1))
                return last

            def transposed(src, done):
                for f in range(KD):
                    for tt in range(TT):
                        last = nc.tensor.transpose(psum[4 + f][:, tt * P:(tt + 1) * P],
                                                   src[:, tt, f * P:(f + 1) * P], ident[:, :])
                    last.then_inc(done, 1)

            def half_bank(bank, tt):
                return psum[bank + tt // 2][:, (tt % 2) * D:(tt % 2 + 1) * D]

            def transpose_t(c):
                pe.wait_ge(uT_lo_ready, at(before(c), 2, 2))
                pe.wait_ge(t_ready, at(c, 4, 4))
                transposed(normed, tT_done)

            def mix_x(c):
                pe.wait_ge(tT_lo_ready, at(c, 2, 2))
                for m in range(KD):
                    product(psum[6 + m][:, :], "x", m, tT_hi, tT_lo).then_inc(wx_done, 1)

            def mix_gates(c):
                pe.wait_ge(xb_lo_ready, at(c, 2, 2))
                for m in range(KD):
                    product(psum[6 + m][:, :], "a", m, mT_hi, mT_lo).then_inc(wa_done, 1)
                for m in range(KD):
                    product(psum[m][:, :], "i", m, mT_hi, mT_lo).then_inc(wi_done, 1)

            def mix_y(c):
                for m in range(KD):
                    pe.wait_ge(tanh_a_ready, at(c, 2, m + 1))
                    product(psum[6 + m][:, :], "y", m, tT_hi, tT_lo).then_inc(wy_done, 1)

            def mix_out(c):
                pe.wait_ge(hy_lo_ready, at(c, 2, 2))
                for tt in range(TT):
                    last = product_by_tokens(half_bank(4, tt), "o", tt, uT_hi, uT_lo)
                    if tt % 2:
                        last.then_inc(wo_done, 1)

            def transpose_u(c):
                pe.wait_ge(u_ready, at(c, 4, 4))
                transposed(normed, uT_done)

            def gate_up(c, m):
                if m == 0:
                    pe.wait_ge(uT_lo_ready, at(c, 2, 2))
                if m >= 2:
                    pe.wait_ge(gu_ready, at(c, 8, m - 1))
                bank = 2 * (m % 2)
                product(psum[bank][:, :], "g", m, uT_hi, uT_lo).then_inc(gate_done, 1)
                product(psum[bank + 1][:, :], "u", m, uT_hi, uT_lo).then_inc(up_done, 1)

            def down(c):
                pe.wait_ge(gu_lo_ready, at(c, 8, 8))
                for tt in range(TT):
                    last = product_by_tokens(half_bank(4, tt), "d", tt, units_hi, units_lo)
                    if tt % 2:
                        last.then_inc(wd_done, 1)

            def transpose_x1(c):
                pe.wait_ge(x1_ready, at(c, 4, 4))
                transposed(row, x1T_done)

            def mlp_up(c, mixing):
                for m in range(KH):
                    if m == 0:
                        pe.wait_ge(x1T_lo_ready, at(c, 2, 2))
                    if m == 2 and mixing:
                        pe.wait_ge(tanh_i_ready, at(after(c), 2, 2))
                    if m >= RING:
                        pe.wait_ge(relu_ready, at(c, 8, m - RING + 1))
                    product(psum[(m + 2) % RING][:, :], "1", m, mT_hi, mT_lo).then_inc(w1_done, 1)

            def mlp_down(c, tiles):
                if tiles[0] == 0:
                    pe.wait_ge(hid_lo_ready, at(c, 8, 8))
                for tt in tiles:
                    last = product_by_tokens(half_bank(6, tt), "2", tt, units_hi, units_lo)
                    if tt % 2:
                        last.then_inc(w2_done, 1)

            def period(c, mixing):
                for m in range(KH - 1):
                    gate_up(c, m)
                if mixing:
                    transpose_t(after(c))
                gate_up(c, KH - 1)
                if mixing:
                    mix_x(after(c))
                down(c)
                if mixing:
                    mix_gates(after(c))
                transpose_x1(c)
                if mixing:
                    mix_y(after(c))
                mlp_up(c, mixing)
                if mixing:
                    mix_out(after(c))
                mlp_down(c, range(TT - 1))
                if mixing:
                    transpose_u(after(c))
                mlp_down(c, range(TT - 1, TT))

            pe.wait_ge(ident_ready, 1)
            pe.wait_ge(vecs_loaded, 6 * DMA)
            nc.tensor.transpose(psum[0][:, 0:NV], vec_rows[:, :], ident[0:NV, 0:NV]).then_inc(vecs_transposed, 1)

            first = (0, 0)
            transpose_t(first)
            pe.wait_ge(lo_split["x"], KD)
            pe.wait_ge(hi_split["x"], KD)
            mix_x(first)
            pe.wait_ge(lo_split["y"], KD)
            pe.wait_ge(hi_split["y"], KD)
            for m in range(KD):
                product(psum[2 + m][:, :], "y", m, tT_hi, tT_lo).then_inc(wy_done, 1)
            for n in ("a", "i"):
                pe.wait_ge(lo_split[n], KD)
                pe.wait_ge(hi_split[n], KD)
            pe.wait_ge(vecs_ready, 1)
            mix_gates(first)
            pe.wait_ge(lo_split["o"], KD)
            pe.wait_ge(hi_split["o"], KD)
            mix_out(first)
            transpose_u(first)
            for n in ("g", "u", "d", "1", "2"):
                pe.wait_ge(lo_split[n], dram[n].shape[0] // P)
                pe.wait_ge(hi_split[n], dram[n].shape[0] // P)

            with pe.Fori(0, CHUNKS // 2 - 1) as pair:
                period((pair, 0), True)
                period((pair, 1), True)
            period((CHUNKS // 2 - 1, 0), True)
            period((CHUNKS // 2 - 1, 1), False)

        @block.scalar
        def _(act):
            def square_x(c):
                pair, k = c
                act.wait_ge(x_loaded[k % 2], pair * DMA + (k // 2 + 1) * DMA)
                for tt in range(TT):
                    last = nc.scalar.activation(normed[:, tt, :], xs[k % 2][:, tt, :], ACT.Square,
                                                accum_out=ss1[:, tt:tt + 1])
                last.then_inc(x_squared, 1)

            def split_hi(dst, bank, done, ready, c):
                for f in range(KD):
                    act.wait_ge(done, at(c, 2, f + 1))
                    nc.scalar.activation(dst[:, f, :], psum[bank + f][:, :], ACT.Copy).then_inc(ready, 1)

            def conv_start(c):
                for m in range(KD):
                    act.wait_ge(wx_done, at(c, 2, m + 1))
                    if m == 0:
                        act.wait_ge(hy_ready, at(before(c), 2, 2))
                    nc.scalar.activation(xv[:, m, LOOKBACK:LOOKBACK + T], psum[6 + m][:, :],
                                         ACT.Copy).then_inc(xraw_ready, 1)
                    nc.scalar.activation(xb[:, m, :], psum[6 + m][:, :], ACT.Identity, bias=vec("cb", m),
                                         scale=vec("cw", LOOKBACK * KD + m)).then_inc(tap_done, 1)

            def xb_hi(c):
                for m in range(KD):
                    act.wait_ge(taps_added, at(c, 6, 4 + m + 1))
                    nc.scalar.activation(mT_hi[:, m, :], xb[:, m, :], ACT.Copy).then_inc(xb_hi_ready, 1)

            def decay_gate(c):
                for m in range(KD):
                    act.wait_ge(wa_done, at(c, 2, m + 1))
                    nc.scalar.activation(decay[:, m, :], psum[6 + m][:, :], ACT.Tanh,
                                         scale=0.5).then_inc(tanh_a_ready, 1)
                for m in range(KD):
                    act.wait_ge(tanh_a_ready, at(c, 2, m + 1))
                    nc.scalar.activation(decay[:, m, :], decay[:, m, :], ACT.Exp, bias=half_c[:, m:m + 1],
                                         scale=half_c[:, m:m + 1]).then_inc(a_ready, 1)

            def square_decay(c):
                act.wait_ge(xtail_saved, at(c, 1, 1))
                for m in range(KD):
                    act.wait_ge(a_ready, at(c, 2, m + 1))
                    nc.scalar.activation(xv[:, m, 0:T], decay[:, m, :], ACT.Square).then_inc(a_squared, 1)

            def input_gate(c):
                for m in range(KD):
                    act.wait_ge(wi_done, at(c, 2, m + 1))
                    nc.scalar.activation(inp[:, m, :], psum[m][:, :], ACT.Tanh,
                                         scale=0.5).then_inc(tanh_i_ready, 1)

            def gate_scale(c):
                for m in range(KD):
                    act.wait_ge(gate_room, at(c, 2, m + 1))
                    nc.scalar.activation(xv[:, m, 0:T], xv[:, m, 0:T], ACT.Sqrt,
                                         scale=-0.25).then_inc(gate_ready, 1)

            def gelu_y(c, bank=6):
                for m in range(KD):
                    act.wait_ge(wy_done, at(c, 2, m + 1))
                    nc.scalar.activation(gy[:, m, :], psum[bank + m][:, :],
                                         ACT.Gelu_apprx_tanh).then_inc(gy_ready, 1)

            def square_h1(c):
                for tt in range(TT):
                    act.wait_ge(h1_ready, at(c, 2, tt // 2 + 1))
                    last = nc.scalar.activation(normed[:, tt, :], h1[:, tt, :], ACT.Square,
                                                accum_out=ss2[:, tt:tt + 1])
                last.then_inc(h1_squared, 1)

            def gelu_gate(c, m):
                act.wait_ge(gate_done, at(c, 8, m + 1))
                if m >= RING:
                    act.wait_ge(gu_lo_ready, at(c, 8, m - RING + 1))
                nc.scalar.activation(ring[:, m % RING, :], psum[2 * (m % 2)][:, :],
                                     ACT.Gelu_apprx_tanh).then_inc(gelu_ready, 1)

            def relu(c, m):
                act.wait_ge(w1_done, at(c, 8, m + 1))
                if m >= RING:
                    act.wait_ge(hid_lo_ready, at(c, 8, m - RING + 1))
                nc.scalar.activation(ring[:, m % RING, :], psum[(m + 2) % RING][:, :], ACT.Relu,
                                     bias=vec("b1", m)).then_inc(relu_ready, 1)

            def period(c, mixing):
                for m in range(KH - 1):
                    gelu_gate(c, m)
                    if m == 1 and mixing:
                        square_x(after(c))
                if mixing:
                    split_hi(tT_hi, 4, tT_done, tT_hi_ready, after(c))
                gelu_gate(c, KH - 1)
                if mixing:
                    conv_start(after(c))
                    xb_hi(after(c))
                    decay_gate(after(c))
                split_hi(mT_hi, 4, x1T_done, x1T_hi_ready, c)
                if mixing:
                    square_decay(after(c))
                    input_gate(after(c))
                    gate_scale(after(c))
                relu(c, 0)
                if mixing:
                    gelu_y(after(c))
                for m in range(1, KH):
                    relu(c, m)
                if mixing:
                    square_h1(after(c))
                    split_hi(uT_hi, 4, uT_done, uT_hi_ready, after(c))

            first = (0, 0)
            square_x(first)
            act.wait_ge(vecs_ready, 1)
            nc.scalar.activation(sp[:, 0, :], vecs[:, VECS["lam"]:VECS["lam"] + KD], ACT.Abs).then_inc(lam_abs, 1)
            act.wait_ge(lam_abs, 1)
            nc.scalar.activation(sp[:, 1, :], sp[:, 0, :], ACT.Exp, scale=-1.0).then_inc(lam_exp, 1)
            split_hi(tT_hi, 4, tT_done, tT_hi_ready, first)
            for n in ("x", "y", "a", "i"):
                act.wait_ge(w_loaded[n], DMA)
                for k in range(KD):
                    if n in "xy":
                        act.wait_ge(vecs_ready, 1)
                        ins = nc.scalar.activation(w_hi[n][:, k, :], raw_w(n, k), ACT.Copy, scale=vec("n1", k))
                    else:
                        ins = nc.scalar.activation(w_hi[n][:, k, :], raw_w(n, k), ACT.Copy)
                    ins.then_inc(hi_split[n], 1)
            conv_start(first)
            gelu_y(first, bank=2)
            xb_hi(first)
            act.wait_ge(consts_ready, 1)
            decay_gate(first)
            square_decay(first)
            input_gate(first)
            gate_scale(first)
            act.preload_act_table(ACT.Gelu_apprx_tanh)
            square_h1(first)
            split_hi(uT_hi, 4, uT_done, uT_hi_ready, first)

            with act.Fori(0, CHUNKS // 2 - 1) as pair:
                period((pair, 0), True)
                period((pair, 1), True)
            period((CHUNKS // 2 - 1, 0), True)
            period((CHUNKS // 2 - 1, 1), False)

        @block.vector
        def _(dve):
            def split_lo(dst, hi, hi_ready, ready, c):
                for f in range(KD):
                    dve.wait_ge(hi_ready, at(c, 2, f + 1))
                    nc.vector.tensor_tensor(dst[:, f, :], psum[4 + f][:, :], hi[:, f, :].bitcast(FP32),
                                            ALU.subtract).then_inc(ready, 1)

            def convolve(c):
                dve.wait_ge(xhead_ready, at(c, 1, 1))
                for step, tap in enumerate(reversed(range(LOOKBACK))):
                    for m in range(KD):
                        if step == 0:
                            dve.wait_ge(xraw_ready, at(c, 2, m + 1))
                            dve.wait_ge(tap_done, at(c, 2, m + 1))
                        else:
                            dve.wait_ge(taps_added, at(c, 6, (step - 1) * KD + m + 1))
                        nc.vector.scalar_tensor_tensor(
                            xb[:, m, :], xv[:, m, tap:tap + T], vec("cw", tap * KD + m), xb[:, m, :],
                            ALU.mult, ALU.add).then_inc(taps_added, 1)

            def xb_lo(c):
                for m in range(KD):
                    dve.wait_ge(xb_hi_ready, at(c, 2, m + 1))
                    nc.vector.tensor_tensor(mT_lo[:, m, :], xb[:, m, :], mT_hi[:, m, :].bitcast(FP32),
                                            ALU.subtract).then_inc(xb_lo_ready, 1)

            def room(c):
                for m in range(KD):
                    dve.wait_ge(a_squared, at(c, 2, m + 1))
                    nc.vector.tensor_scalar(xv[:, m, 0:T], xv[:, m, 0:T], 1.0, -GATE_FLOOR, ALU.subtract,
                                            ALU.min).then_inc(gate_room, 1)

            def scan_input(c):
                for m in range(KD):
                    dve.wait_ge(tanh_i_ready, at(c, 2, m + 1))
                    nc.vector.scalar_tensor_tensor(inp[:, m, :], inp[:, m, :], 1.0, xb[:, m, :], ALU.add,
                                                   ALU.mult).then_inc(ix_ready, 1)
                for m in range(KD):
                    dve.wait_ge(gate_ready, at(c, 2, m + 1))
                    dve.wait_ge(ix_ready, at(c, 2, m + 1))
                    nc.vector.tensor_tensor(inp[:, m, :], inp[:, m, :], xv[:, m, 0:T],
                                            ALU.mult).then_inc(b_ready, 1)

            def scan(c, m):
                begins = c[1] % 2 == 0
                if not begins:
                    dve.wait_ge(h_saved, at(before(c), 2, 2))
                dve.wait_ge(b_ready, at(c, 2, m + 1))
                nc.vector.tensor_tensor_scan(xv[:, m, 0:T], decay[:, m, :], inp[:, m, :],
                                             0.0 if begins else h_last[:, m:m + 1],
                                             ALU.mult, ALU.add).then_inc(h_ready, 1)

            def gated(c):
                for m in range(KD):
                    dve.wait_ge(h_ready, at(c, 2, m + 1))
                    nc.vector.tensor_copy(h_last[:, m:m + 1], xv[:, m, T - 1:T]).then_inc(h_saved, 1)
                    dve.wait_ge(gy_ready, at(c, 2, m + 1))
                    nc.vector.tensor_tensor(gy[:, m, :], gy[:, m, :], xv[:, m, 0:T],
                                            ALU.mult).then_inc(hy_ready, 1)

            def hy_lo(c):
                for m in range(KD):
                    dve.wait_ge(hy_hi_ready, at(c, 2, m + 1))
                    nc.vector.tensor_tensor(uT_lo[:, m, :], gy[:, m, :], uT_hi[:, m, :].bitcast(FP32),
                                            ALU.subtract).then_inc(hy_lo_ready, 1)

            def add_mix(c):
                for q in range(PAIRS):
                    dve.wait_ge(wo_done, at(c, 2, q + 1))
                    nc.vector.tensor_tensor(h1[:, 2 * q:2 * q + 2, :].rearrange("p t d -> p (t d)"),
                                            psum[4 + q][:, :],
                                            xs[c[1] % 2][:, 2 * q:2 * q + 2, :].rearrange("p t d -> p (t d)"),
                                            ALU.add).then_inc(h1_ready, 1)

            def statistics(c, i, q, sum_ready):
                dve.wait_ge(sum_ready, at(c, 2, q + 1))
                for tt in (2 * q, 2 * q + 1):
                    nc.vector.bn_stats(ln_stats[:, tt, :], row[:, tt, :]).then_inc(bn_done[i], 1)
                for tt in (2 * q, 2 * q + 1):
                    dve.wait_ge(bn_done[i], at(c, 4, tt + 1))
                    dve.sem_inc(dve_carried, 1)
                    last = nc.vector.bn_aggr(ln_mv[:, tt, :], ln_stats[:, tt, :])
                last.then_inc(mv_done[i], 1)

            def normalise(c, i, q, ready):
                dve.wait_ge(ln_rstd_ready[i], at(c, 2, q + 1))
                for tt in (2 * q, 2 * q + 1):
                    nc.vector.tensor_scalar(row[:, tt, :], row[:, tt, :], ln_mv[:, tt, 0:1],
                                            ln_rstd[:, tt:tt + 1], ALU.subtract, ALU.mult).then_inc(ready, 1)

            def first_sum(c, q):
                dve.wait_ge(wd_done, at(c, 2, q + 1))
                if q == 0:
                    dve.wait_ge(xh_ready, at(c, 2, 2))
                    dve.wait_ge(out_stored, at(c, 2 * DMA, DMA))
                nc.vector.tensor_tensor(row[:, 2 * q:2 * q + 2, :].rearrange("p t d -> p (t d)"),
                                        psum[4 + q][:, :],
                                        xs[c[1] % 2][:, 2 * q:2 * q + 2, :].rearrange("p t d -> p (t d)"),
                                        ALU.add).then_inc(s1_ready, 1)

            def second_sum(c, q):
                dve.wait_ge(w2_done, at(c, 2, q + 1))
                dve.wait_ge(b2_added, at(c, 4, 2 * q + 2))
                flat = row[:, 2 * q:2 * q + 2, :].rearrange("p t d -> p (t d)")
                nc.vector.tensor_tensor(flat, psum[6 + q][:, :], flat, ALU.add).then_inc(s2_ready, 1)

            def gate_times_up(c, m):
                dve.wait_ge(gelu_ready, at(c, 8, m + 1))
                dve.wait_ge(up_done, at(c, 8, m + 1))
                nc.vector.tensor_tensor(ring[:, m % RING, :], psum[2 * (m % 2) + 1][:, :],
                                        ring[:, m % RING, :], ALU.mult).then_inc(gu_ready, 1)

            def unit_lo(c, m, hi_ready, ready):
                dve.wait_ge(hi_ready, at(c, 8, m + 1))
                nc.vector.tensor_tensor(units_lo[:, m, :], ring[:, m % RING, :],
                                        units_hi[:, m, :].bitcast(FP32), ALU.subtract).then_inc(ready, 1)

            def period(c, mixing):
                n = after(c)
                for m in range(KH):
                    gate_times_up(c, m)
                    if m:
                        unit_lo(c, m - 1, gu_hi_ready, gu_lo_ready)
                    if m == KH - 2 and mixing:
                        split_lo(tT_lo, tT_hi, tT_hi_ready, tT_lo_ready, n)
                unit_lo(c, KH - 1, gu_hi_ready, gu_lo_ready)
                if mixing:
                    convolve(n)
                first_sum(c, 0)
                statistics(c, 0, 0, s1_ready)
                if mixing:
                    xb_lo(n)
                normalise(c, 0, 0, x1_ready)
                first_sum(c, 1)
                statistics(c, 0, 1, s1_ready)
                normalise(c, 0, 1, x1_ready)
                split_lo(mT_lo, mT_hi, x1T_hi_ready, x1T_lo_ready, c)
                if mixing:
                    room(n)
                    scan_input(n)
                    scan(n, 0)
                    scan(n, 1)
                unit_lo(c, 0, hid_hi_ready, hid_lo_ready)
                if mixing:
                    gated(n)
                unit_lo(c, 1, hid_hi_ready, hid_lo_ready)
                if mixing:
                    hy_lo(n)
                for m in range(2, KH):
                    unit_lo(c, m, hid_hi_ready, hid_lo_ready)
                if mixing:
                    add_mix(n)
                second_sum(c, 0)
                statistics(c, 1, 0, s2_ready)
                normalise(c, 1, 0, out_ready)
                if mixing:
                    split_lo(uT_lo, uT_hi, uT_hi_ready, uT_lo_ready, n)
                second_sum(c, 1)
                statistics(c, 1, 1, s2_ready)
                normalise(c, 1, 1, out_ready)

            def weight_lo(n, norm=None):
                for k in range(dram[n].shape[0] // P):
                    dve.wait_ge(hi_split[n], k + 1)
                    hi = w_hi[n][:, k, :].bitcast(FP32)
                    if norm:
                        ins = nc.vector.scalar_tensor_tensor(w_lo[n][:, k, :], raw_w(n, k), vec(norm, k), hi,
                                                             ALU.mult, ALU.subtract)
                    else:
                        ins = nc.vector.tensor_tensor(w_lo[n][:, k, :], raw_w(n, k), hi, ALU.subtract)
                    ins.then_inc(lo_split[n], 1)

            steps = 0

            def lam_stepped(ins):
                nonlocal steps
                steps += 1
                ins.then_inc(lam_step, 1)
                dve.wait_ge(lam_step, steps)

            dve.wait_ge(vecs_transposed, 1)
            nc.vector.tensor_copy(vecs[:, :], psum[0][:, 0:NV]).then_inc(vecs_ready, 1)
            dve.wait_ge(vecs_ready, 1)
            lams = vecs[:, VECS["lam"]:VECS["lam"] + KD]
            e, z, s, poly = (sp[:, i, :] for i in (1, 2, 3, 4))
            dve.wait_ge(lam_exp, 1)
            lam_stepped(nc.vector.tensor_scalar(z, e, 2.0, None, ALU.add))
            lam_stepped(nc.vector.reciprocal(s, z))
            lam_stepped(nc.vector.tensor_tensor(s, s, e, ALU.mult))
            lam_stepped(nc.vector.tensor_tensor(z, s, s, ALU.mult))
            lam_stepped(nc.vector.tensor_scalar(poly, z, 1.0 / 17.0, None, ALU.mult))
            for odd in range(15, 1, -2):
                lam_stepped(nc.vector.scalar_tensor_tensor(poly, poly, 1.0 / odd, z, ALU.add, ALU.mult))
            lam_stepped(nc.vector.scalar_tensor_tensor(poly, poly, 1.0, s, ALU.add, ALU.mult))
            lam_stepped(nc.vector.tensor_scalar(z, lams, 0.0, -0.5 * C_CONST, ALU.max, ALU.mult))
            nc.vector.scalar_tensor_tensor(half_c[:, :], poly, -C_CONST, z, ALU.mult,
                                           ALU.add).then_inc(consts_ready, 1)

            first = (0, 0)
            split_lo(tT_lo, tT_hi, tT_hi_ready, tT_lo_ready, first)
            for n in ("x", "y"):
                weight_lo(n, "n1")
            for n in ("a", "i"):
                weight_lo(n)
            convolve(first)
            xb_lo(first)
            for n in ("g", "u"):
                weight_lo(n, "n2")
            weight_lo("o")
            room(first)
            weight_lo("d")
            scan_input(first)
            for m in range(KD):
                scan(first, m)
            gated(first)
            hy_lo(first)
            weight_lo("1")
            add_mix(first)
            weight_lo("2")
            split_lo(uT_lo, uT_hi, uT_hi_ready, uT_lo_ready, first)

            with dve.Fori(0, CHUNKS // 2 - 1) as pair:
                period((pair, 0), True)
                period((pair, 1), True)
            period((CHUNKS // 2 - 1, 0), True)
            period((CHUNKS // 2 - 1, 1), False)

        @block.gpsimd
        def _(pool):
            def carry():
                pool.sem_inc(pool_carried, 1)

            def rms(c, ss, squared, ms_done, rstd, rstd_ready):
                pool.wait_ge(squared, at(c, 1, 1))
                carry()
                nc.gpsimd.tensor_scalar(rstd[:, :], ss[:, :], 1.0 / D, RMS_EPS, ALU.mult,
                                        ALU.add).then_inc(ms_done, 1)
                pool.wait_ge(ms_done, at(c, 1, 1))
                nc.gpsimd.tensor_tensor(rstd[:, :], rstd[:, :], minus_half[:, :], ALU.pow).then_inc(rstd_ready, 1)

            def norm_t(c):
                rms(c, ss1, x_squared, rms1_ms, rstd1, rms1_rstd)
                pool.wait_ge(uT_done, at(before(c), 2, 2))
                pool.wait_ge(rms1_rstd, at(c, 1, 1))
                carry()
                for tt in range(TT):
                    nc.gpsimd.tensor_scalar(normed[:, tt, :], xs[c[1] % 2][:, tt, :], rstd1[:, tt:tt + 1], 0.0,
                                            ALU.mult, ALU.add).then_inc(t_ready, 1)

            def head(c):
                pool.wait_ge(hy_ready, at(before(c), 2, 2))
                carry()
                if c[1] % 2 == 0:
                    nc.gpsimd.memset(xv[:, :, 0:LOOKBACK], 0.0).then_inc(xhead_ready, 1)
                else:
                    pool.wait_ge(xtail_saved, at(before(c), 1, 1))
                    carry()
                    nc.gpsimd.tensor_copy(xv[:, :, 0:LOOKBACK], xtail[:, :, :]).then_inc(xhead_ready, 1)

            def tail(c):
                pool.wait_ge(xhead_ready, at(c, 1, 1))
                pool.wait_ge(xraw_ready, at(c, 2, 2))
                carry()
                nc.gpsimd.tensor_copy(xtail[:, :, :], xv[:, :, T:T + LOOKBACK]).then_inc(xtail_saved, 1)

            def hy_hi(c, m):
                pool.wait_ge(hy_ready, at(c, 2, m + 1))
                carry()
                nc.gpsimd.tensor_scalar(uT_hi[:, m, :], gy[:, m, :], 1.0, 0.0, ALU.mult,
                                        ALU.add).then_inc(hy_hi_ready, 1)

            def norm_u(c):
                rms(c, ss2, h1_squared, rms2_ms, rstd2, rms2_rstd)
                pool.wait_ge(rms2_rstd, at(c, 1, 1))
                carry()
                for tt in range(TT):
                    nc.gpsimd.tensor_scalar(normed[:, tt, :], h1[:, tt, :], rstd2[:, tt:tt + 1], 0.0,
                                            ALU.mult, ALU.add).then_inc(u_ready, 1)

            def add_x_h1(c):
                for q in range(PAIRS):
                    x_pair = xs[c[1] % 2][:, 2 * q:2 * q + 2, :]
                    nc.gpsimd.tensor_tensor(x_pair, x_pair, h1[:, 2 * q:2 * q + 2, :],
                                            ALU.add).then_inc(xh_ready, 1)

            def ln_scale(c, i, q):
                pool.wait_ge(mv_done[i], at(c, 2, q + 1))
                pair_rstd = ln_rstd[:, 2 * q:2 * q + 2]
                carry()
                nc.gpsimd.tensor_scalar(pair_rstd, ln_mv[:, 2 * q:2 * q + 2, 1], 1.0, LN_EPS, ALU.mult,
                                        ALU.add).then_inc(ve_done[i], 1)
                pool.wait_ge(ve_done[i], at(c, 2, q + 1))
                nc.gpsimd.tensor_tensor(pair_rstd, pair_rstd, minus_half[:, 0:2],
                                        ALU.pow).then_inc(ln_rstd_ready[i], 1)

            def add_b2(c):
                for tt in range(TT):
                    pool.wait_ge(x1T_done, at(c, 2, 2))
                    nc.gpsimd.tensor_tensor(row[:, tt, :], row[:, tt, :], b2_rows[:, :],
                                            ALU.add).then_inc(b2_added, 1)

            def unit_hi(c, m, unit_ready, ready):
                pool.wait_ge(unit_ready, at(c, 8, m + 1))
                carry()
                nc.gpsimd.tensor_scalar(units_hi[:, m, :], ring[:, m % RING, :], 1.0, 0.0, ALU.mult,
                                        ALU.add).then_inc(ready, 1)

            def period(c, mixing):
                n = after(c)
                for m in range(KH):
                    unit_hi(c, m, gu_ready, gu_hi_ready)
                    if m == 2 and mixing:
                        norm_t(n)
                        head(n)
                if mixing:
                    tail(n)
                ln_scale(c, 0, 0)
                ln_scale(c, 0, 1)
                add_b2(c)
                unit_hi(c, 0, relu_ready, hid_hi_ready)
                unit_hi(c, 1, relu_ready, hid_hi_ready)
                if mixing:
                    hy_hi(n, 0)
                    hy_hi(n, 1)
                for m in range(2, KH):
                    unit_hi(c, m, relu_ready, hid_hi_ready)
                if mixing:
                    norm_u(n)
                ln_scale(c, 1, 0)
                if mixing:
                    add_x_h1(n)
                ln_scale(c, 1, 1)

            def weight_hi(n, norm=None):
                width = dram[n].shape[1]
                pool.wait_ge(w_loaded[n], DMA)
                for k in range(dram[n].shape[0] // P):
                    nc.gpsimd.tensor_scalar(w_hi[n][:, k, :], raw_w(n, k), vec(norm, k) if norm else 1.0, 0.0,
                                            ALU.mult, ALU.add).then_inc(hi_split[n], 1)

            nc.gpsimd.memset(ident[:, :], 0.0).then_inc(ident_zero, 1)
            nc.gpsimd.memset(minus_half[:, :], -0.5)
            pool.wait_ge(ident_zero, 1)
            nc.gpsimd.affine_select(out=ident[:, :], in_=ident[:, :], compare_op=ALU.not_equal, fill=1.0,
                                    base=0, pattern=[[-1, P]], channel_multiplier=1).then_inc(ident_ready, 1)
            first = (0, 0)
            norm_t(first)
            head(first)
            tail(first)
            pool.wait_ge(vecs_ready, 1)
            for n in ("g", "u"):
                weight_hi(n, "n2")
            for n in ("o", "d", "1", "2"):
                weight_hi(n)
            for m in range(KD):
                hy_hi(first, m)
            norm_u(first)
            add_x_h1(first)
            pool.wait_ge(b2_loaded, DMA)
            for n in ("g", "u", "d", "1", "2"):
                pool.wait_ge(lo_split[n], dram[n].shape[0] // P)

            with pool.Fori(0, CHUNKS // 2 - 1) as pair:
                period((pair, 0), True)
                period((pair, 1), True)
            period((CHUNKS // 2 - 1, 0), True)
            period((CHUNKS // 2 - 1, 1), False)


_INS = ["L0_attn_x", "L0_attn_norm1_w", "L0_attn_Wx", "L0_attn_Wy", "L0_attn_conv_w", "L0_attn_conv_b",
        "L0_attn_Wi", "L0_attn_Wa", "L0_attn_lam", "L0_attn_Wo", "L0_attn_norm2_w", "L0_attn_Wg",
        "L0_attn_Wu", "L0_attn_Wd", "L0_ffn_W1", "L0_ffn_b1", "L0_ffn_W2", "L0_ffn_b2"]
_OUTS = [((4, 1024, 256), "float32")]


def kernel(**inputs):
    import numpy as _np
    import concourse.bacc as _bacc
    from concourse import mybir as _mybir
    from concourse.bass_utils import run_bass_kernel_spmd as _run

    nc = _bacc.Bacc("TRN2", target_bir_lowering=False, num_devices=1)
    arrays, args = {}, []
    for name in _INS:
        a = _np.ascontiguousarray(inputs[name])
        arrays[f"in_{name}_dram"] = a
        args.append(nc.dram_tensor(f"in_{name}_dram", a.shape, _mybir.dt.from_np(a.dtype), kind="ExternalInput").ap())
    for i, (shape, dtype) in enumerate(_OUTS):
        dt = _mybir.dt.from_np(_np.dtype(dtype))
        args.append(nc.dram_tensor(f"out_{i}_dram", shape, dt, kind="ExternalOutput").ap())
    griffin_mlp_kernel(nc, *args)
    r = _run(nc, [arrays], core_ids=[0])
    got = tuple(r.results[0][f"out_{i}_dram"] for i in range(len(_OUTS)))
    return got[0]
```
